# Optimizing a Trainium2 kernel written in Bass

```python
import numpy as np
import jax
import jax.numpy as jnp

def _softmax(x, axis=-1):
    return jax.nn.softmax(x, axis=axis)

def _gelu(x):
    return jax.nn.gelu(x, approximate=True)

def _silu(x):
    return jax.nn.silu(x)

def _sigmoid(x):
    return jax.nn.sigmoid(x)

def _layernorm(x, axis=-1, eps=1e-05):
    m = jnp.mean(x, axis=axis, keepdims=True)
    v = jnp.var(x, axis=axis, keepdims=True)
    return (x - m) / jnp.sqrt(v + eps)

def _scatter_add(tgt, idx, src, axis=0):
    return tgt.at[idx].add(src)

def _segment_sum(src, seg, n):
    return jax.ops.segment_sum(src, seg, n)
kernel_name = 'mk_adj_resnorm_d1_adj_r2_a5696c'

def setup_inputs(seed: int=0):
    np.random.seed(seed)
    _w = jnp.asarray

    def _rec_inputs():
        import jax
        import jax.numpy as jnp
        _gk = jax.random.key(seed)
        x = -0.0005207 + 1.001 * jax.random.normal(jax.random.fold_in(_gk, 1), (4096, 128), jnp.float32)
        _a = jax.random.bernoulli(jax.random.fold_in(_gk, 2), 0.000488281, (4096, 4096))
        _a = jnp.logical_or(_a, jnp.swapaxes(_a, -1, -2))
        _a = jnp.logical_or(_a, jnp.eye(4096, dtype=bool))
        _af = _a.astype(jnp.float32)
        _af = _af * jax.random.uniform(jax.random.fold_in(_gk, 3), (4096, 4096), jnp.float32, 0.05, 5.41998)
        adj = _af
        return (x, adj)
    x, adj = _rec_inputs()

    def _L0_gnn_setup():
        import jax, jax.numpy as jnp
        import numpy as np
        N = 4096
        C = 128
        key = jax.random.key(seed)
        k1, k2, k3 = jax.random.split(key, 3)
        x = jax.random.normal(k1, (N, C), dtype=jnp.float32)
        evals = jax.random.uniform(k2, (N,), dtype=jnp.float32)
        evecs = jax.random.normal(k3, (N, N), dtype=jnp.float32)
        t = jnp.ones((1,), dtype=jnp.float32)
        return {'x': x, 'evals': evals, 'evecs': evecs, 't': t}
    _L0_gnn_all = _L0_gnn_setup()
    _L0_gnn_in = {k: v for k, v in _L0_gnn_all.items() if k in ('evals', 't')}
    del _L0_gnn_all
    return {'x': x, 'adj': adj, 'L0_gnn_evals': _L0_gnn_in['evals'], 'L0_gnn_t': _L0_gnn_in['t']}

def reference(x, adj, L0_gnn_evals, L0_gnn_t):
    import jax
    import jax.numpy as jnp

    def _L0_gnn_ref(x, evals, evecs, t):
        import jax, jax.numpy as jnp
        import numpy as np
        N = 4096
        C = 128
        t_eff = jnp.clip(t[0], 1e-08, None)
        x_spec = jnp.einsum('nk,nc->kc', evecs, x)
        coefs = jnp.exp(-evals * t_eff)[:, None]
        out = jnp.einsum('nk,kc->nc', evecs, coefs * x_spec)
        return out
    x = _layernorm(x + _L0_gnn_ref(x, L0_gnn_evals, adj, L0_gnn_t), axis=-1)
    return x

_drawn_inputs = setup_inputs


def setup_inputs(seed=0):
    import zlib

    import numpy as np

    out = dict(_drawn_inputs(seed))
    spreads = {}
    factors = {}
    for name, (base, spread) in spreads.items():
        noise = np.random.default_rng([zlib.crc32(name.encode()), seed]).standard_normal(out[name].shape)
        drawn = base * np.exp(spread * noise) if base else spread * noise
        out[name] = jnp.asarray(drawn.astype(out[name].dtype))
    for name, factor in factors.items():
        out[name] = (out[name] * factor).astype(out[name].dtype)
    return out
```

```python
from contextlib import ExitStack

import concourse.bass as bass
from concourse import mybir

F32 = mybir.dt.float32
F32R = mybir.dt.float32r
ALU = mybir.AluOpType
ACT = mybir.ActivationFunctionType

P = 128
W = 512
U = W // P
SLOTS = 16
EPS = 1e-5
T_MIN = 1e-8


def heat_layernorm(nc: bass.Bass, x: bass.AP, adj: bass.AP, evals: bass.AP, t: bass.AP, out: bass.AP):
    N, C = x.shape
    G = N // W
    B = N // W
    GROUPS = B * G
    LAG = G + 1
    KT = N // P
    TURNS = (GROUPS - LAG) // SLOTS
    LOOPED = TURNS * SLOTS
    assert C == P and N % W == 0 and SLOTS == 2 * G and B % 2 == 0

    x_rows = x.rearrange("(g p u) c -> g p u c", p=P, u=U)
    out_rows = out.rearrange("(g p u) c -> g p u c", p=P, u=U)
    adj_rows = adj.rearrange("(g p u) k -> g p u k", p=P, u=U)

    with ExitStack() as ctx:
        def sb(name, shape, dt=F32):
            return ctx.enter_context(nc.sbuf_tensor(name, shape, dt))

        def sem(name):
            return ctx.enter_context(nc.semaphore(name))

        adj_sb = sb("adj_sb", [P, SLOTS, U, W])
        x_hi = sb("x_hi", [P, G, U, C], F32R)
        x_lo = sb("x_lo", [P, G, U, C], F32R)
        acc = sb("acc", [P, G, W])
        hi = sb("hi", [P, 4, W], F32R)
        lo = sb("lo", [P, 4, W], F32R)
        y_sb = sb("y_sb", [P, W])
        s_hi = sb("s_hi", [P, 2, U, C], F32R)
        s_lo = sb("s_lo", [P, 2, U, C], F32R)
        ident = sb("ident", [P, P])
        evals_sb = sb("evals_sb", [KT, P])
        t_sb = sb("t_sb", [KT, 1])
        neg_t = sb("neg_t", [KT, 1])
        coef_rows = sb("coef_rows", [KT, P])
        coef = sb("coef", [P, KT])
        eps_sb = sb("eps_sb", [P, 1])
        stats = sb("stats", [P, U, 6])
        mean_var = sb("mean_var", [P, 2, U, 2])
        std = sb("std", [P, 2, U])
        rstd = sb("rstd", [P, 2, U])
        shift = sb("shift", [P, 2, U])

        y_ps = ctx.enter_context(nc.psum_tensor("y_ps", [P, 2, W], F32))
        o_ps = ctx.enter_context(nc.psum_tensor("o_ps", [P, 2, W], F32))
        at_ps = ctx.enter_context(nc.psum_tensor("at_ps", [P, U, W], F32))

        x_loaded = [sem(f"x_loaded{g}") for g in range(G)]
        adj_loaded = [sem(f"adj_loaded{k}") for k in range(SLOTS)]
        spectrum_loaded = sem("spectrum_loaded")
        out_stored = sem("out_stored")
        ident_zeroed = sem("ident_zeroed")
        ident_ready = sem("ident_ready")
        t_clipped = sem("t_clipped")
        t_ready = sem("t_ready")
        eps_ready = sem("eps_ready")
        coef_rows_ready = sem("coef_rows_ready")
        coef_transposed = sem("coef_transposed")
        coef_ready = sem("coef_ready")
        x_hi_ready = sem("x_hi_ready")
        x_lo_ready = sem("x_lo_ready")
        x_transposed = sem("x_transposed")
        a_hi_ready = sem("a_hi_ready")
        a_lo_ready_dve = sem("a_lo_ready_dve")
        a_lo_ready_pool = sem("a_lo_ready_pool")
        first_done = sem("first_done")
        at_transposed = sem("at_transposed")
        at_hi_ready = sem("at_hi_ready")
        at_lo_ready = sem("at_lo_ready")
        second_done = sem("second_done")
        acc_written = sem("acc_written")
        y_copied = sem("y_copied")
        y_transposed = sem("y_transposed")
        s_scaled = sem("s_scaled")
        s_hi_ready = sem("s_hi_ready")
        s_ready = sem("s_ready")
        rows_transposed = sem("rows_transposed")
        stats_ready = sem("stats_ready")
        mean_var_ready = sem("mean_var_ready")
        std_ready = sem("std_ready")
        rstd_ready = sem("rstd_ready")
        shift_ready = sem("shift_ready")
        rows_ready = sem("rows_ready")

        PROLOGUE = LAG * U

        TAIL = (GROUPS - LAG) * U

        def first_buffer(n):
            return n % 4 if n < PROLOGUE else n % 2

        def second_buffer(m):
            return m % 4 if m >= TAIL else 2 + m % 2

        def ahead(m):
            return 2 if m >= TAIL else 1

        def transposes_ahead(m):
            return 3 if m >= TAIL else 1

        def finished(i):
            return i - LAG - 1 - (GROUPS - G)

        def starts_block(i):
            return i % G == 0 and G <= i <= GROUPS

        block = ctx.enter_context(nc.Block())

        @block.sync
        def _(sp):
            def load(slot, g, b):
                return sp.dma_start(adj_sb[:, slot], adj_rows[g, :, :, bass.ts(b, W)]).then_inc(adj_loaded[slot], 16)

            for i in range(SLOTS):
                if i < G:
                    sp.dma_start(acc[:, i].rearrange("p (u c) -> p u c", u=U), x_rows[i]).then_inc(x_loaded[i], 16)
                load(i, i % G, i // G)
            with sp.Fori(0, GROUPS // SLOTS - 1) as turn:
                for v in range(SLOTS):
                    sp.wait_ge(at_transposed, turn * (SLOTS * U) + (v + 1) * U)
                    load(v, v % G, turn * 2 + (2 + v // G))
            for g in range(G):
                sp.wait_ge(rows_ready, U * (g + 1))
                sp.dma_start(out_rows[g], adj_sb[:, g, 0].rearrange("p (u c) -> p u c", u=U)).then_inc(out_stored, 16)
            sp.wait_ge(out_stored, 16 * G)

        @block.gpsimd
        def _(pool):
            pool.memset(ident[:], 0.0).then_inc(ident_zeroed, 1)
            pool.wait_ge(ident_zeroed, 1)
            pool.affine_select(out=ident[:], in_=ident[:], compare_op=ALU.not_equal, fill=1.0, base=0,
                               pattern=[[-1, P]], channel_multiplier=1).then_inc(ident_ready, 1)

            def split_low(n, at):
                pool.wait_ge(a_hi_ready, at + 1)
                pool.tensor_tensor(lo[:, first_buffer(n)], adj_sb[:, n // U % SLOTS, n % U], hi[:, first_buffer(n)].bitcast(F32),
                                   ALU.subtract).then_inc(a_lo_ready_pool, 1)

            with pool.Fori(0, TURNS) as turn:
                for n in range(PROLOGUE, PROLOGUE + SLOTS * U):
                    split_low(n, turn * (SLOTS * U) + n)
            for n in range(PROLOGUE + LOOPED * U, GROUPS * U):
                split_low(n, n)

        @block.scalar
        def _(act):
            act.dma_start(evals_sb[:], evals.rearrange("(k p) -> k p", p=P)).then_inc(spectrum_loaded, 16)
            act.dma_start(t_sb[:], t.rearrange("(a b) -> a b", a=1).to_broadcast([KT, 1])).then_inc(spectrum_loaded, 16)
            act.wait_ge(spectrum_loaded, 32)
            act.wait_ge(t_ready, 1)
            act.activation(coef_rows[:], evals_sb[:], ACT.Exp, scale=neg_t[:]).then_inc(coef_rows_ready, 1)

            def split_high(n, turn=0):
                i = n // U
                if n % U == 0:
                    act.wait_ge(adj_loaded[i % SLOTS], turn * 16 + 16 * (i // SLOTS + 1))
                if n >= PROLOGUE:
                    act.wait_ge(first_done, turn * (SLOTS * U) + (n - 1))
                elif n >= 4:
                    act.wait_ge(first_done, n - 3)
                act.activation(hi[:, first_buffer(n)], adj_sb[:, i % SLOTS, n % U], ACT.Copy).then_inc(a_hi_ready, 1)

            def split_high_transposed(m, turn=0):
                act.wait_ge(at_transposed, turn * (SLOTS * U) + (m + 1))
                if m == TAIL:
                    act.wait_ge(first_done, GROUPS * U)
                if m >= TAIL + 4:
                    act.wait_ge(second_done, m - 3)
                elif m >= TAIL:
                    act.wait_ge(second_done, TAIL)
                elif m >= 2:
                    act.wait_ge(second_done, turn * (SLOTS * U) + (m - 1))
                act.activation(hi[:, second_buffer(m)], at_ps[:, m % U], ACT.Copy).then_inc(at_hi_ready, 1)

            def copy_y(b, turn=0):
                act.wait_ge(first_done, turn * (SLOTS * U) + G * U * (b + 1))
                if b >= 1:
                    act.wait_ge(s_ready, turn * 2 + b)
                act.activation(y_sb[:], y_ps[:, b % 2], ACT.Copy).then_inc(y_copied, 1)

            def split_s_high(b, turn=0):
                act.wait_ge(s_scaled, turn * 2 + (b + 1))
                if b >= 2:
                    act.wait_ge(second_done, turn * (SLOTS * U) + G * U * (b - 1))
                act.activation(s_hi[:, b % 2], y_sb[:].rearrange("p (u c) -> p u c", u=U), ACT.Copy).then_inc(s_hi_ready, 1)

            def step(i, turn=0):
                j = i - LAG
                for u in range(U):
                    if i < GROUPS:
                        split_high(i * U + u, turn)
                    if starts_block(i) and u == 1:
                        copy_y(i // G - 1, turn)
                    if j >= 0:
                        split_high_transposed(j * U + u, turn)
                    if starts_block(i) and u == 3:
                        split_s_high(i // G - 1, turn)
                    if u == 1 and finished(i) >= 1:
                        deviation(finished(i) - 1)
                    if u == 3 and finished(i) >= 1:
                        normalise(finished(i) - 1)

            def deviation(g):
                act.wait_ge(mean_var_ready, g + 1)
                if g >= 2:
                    act.wait_ge(rstd_ready, g - 1)
                act.activation(std[:, g % 2], mean_var[:, g % 2, :, 1], ACT.Sqrt, bias=eps_sb[:]).then_inc(std_ready, 1)

            def normalise(g):
                act.wait_ge(shift_ready, g + 1)
                for u in range(U):
                    act.activation(adj_sb[:, g, 0, u * C:(u + 1) * C], y_ps[:, g % 2, u * C:(u + 1) * C], ACT.Identity,
                                   scale=rstd[:, g % 2, u:u + 1], bias=shift[:, g % 2, u:u + 1]).then_inc(rows_ready, 1)

            for g in range(G):
                act.wait_ge(x_loaded[g], 16)
                act.activation(x_hi[:, g], acc[:, g].rearrange("p (u c) -> p u c", u=U), ACT.Copy).then_inc(x_hi_ready, 1)
                step(g)
            step(G)
            with act.Fori(0, TURNS) as turn:
                for i in range(LAG, LAG + SLOTS):
                    step(i, turn)
            act.wait_ge(eps_ready, 1)
            for i in range(LAG + LOOPED, GROUPS + LAG):
                step(i)
            deviation(G - 2)
            normalise(G - 2)
            deviation(G - 1)
            normalise(G - 1)

        @block.vector
        def _(dve):
            dve.memset(eps_sb[:], EPS).then_inc(eps_ready, 1)
            dve.wait_ge(spectrum_loaded, 32)
            dve.tensor_scalar(neg_t[:], t_sb[:], T_MIN, -1.0, ALU.max, ALU.mult).then_inc(t_ready, 1)

            def split_low_transposed(m, turn=0):
                dve.wait_ge(at_hi_ready, turn * (SLOTS * U) + (m + 1))
                dve.tensor_tensor(lo[:, second_buffer(m)], at_ps[:, m % U], hi[:, second_buffer(m)].bitcast(F32),
                                  ALU.subtract).then_inc(at_lo_ready, 1)

            def accumulate(j, turn=0):
                dve.wait_ge(second_done, turn * (SLOTS * U) + U * (j + 1))
                dve.tensor_tensor(acc[:, j % G], o_ps[:, j % 2], acc[:, j % G], ALU.add).then_inc(acc_written, 1)

            def scale_s(b, turn=0):
                dve.wait_ge(y_transposed, turn * 2 + (b + 1))
                c = coef[:, bass.ds(turn * (2 * U) + b * U, U)].unsqueeze(2).to_broadcast([P, U, C])
                dve.tensor_tensor(y_sb[:].rearrange("p (u c) -> p u c", u=U),
                                  y_ps[:, b % 2].rearrange("p (u c) -> p u c", u=U), c, ALU.mult).then_inc(s_scaled, 1)

            def split_s_low(b, turn=0):
                dve.wait_ge(s_hi_ready, turn * 2 + (b + 1))
                dve.tensor_tensor(s_lo[:, b % 2], y_sb[:].rearrange("p (u c) -> p u c", u=U),
                                  s_hi[:, b % 2].bitcast(F32), ALU.subtract).then_inc(s_ready, 1)

            def step(i, turn=0):
                j = i - LAG
                for u in range(U):
                    m = j * U + u
                    if starts_block(i) and u == 2:
                        scale_s(i // G - 1, turn)
                    if starts_block(i) and u == 3:
                        split_s_low(i // G - 1, turn)
                    if u == 0 and finished(i) >= 1:
                        shift_and_scale(finished(i) - 1)
                    if u == 3 and finished(i) >= 0:
                        statistics(finished(i))
                    if m == TAIL:
                        split_low_transposed(m + 1)
                    if j >= 0 and m + ahead(m) < GROUPS * U:
                        split_low_transposed(m + ahead(m), turn)
                if j >= 0:
                    accumulate(j, turn)

            def statistics(g):
                dve.wait_ge(rows_transposed, g + 1)
                for u in range(U):
                    dve.bn_stats(stats[:, u], y_ps[:, g % 2, u * C:(u + 1) * C]).then_inc(stats_ready, 1)
                dve.wait_ge(stats_ready, U * (g + 1))
                if g >= 2:
                    dve.wait_ge(std_ready, g - 1)
                for u in range(U):
                    last = dve.bn_aggr(mean_var[:, g % 2, u], stats[:, u])
                last.then_inc(mean_var_ready, 1)

            def shift_and_scale(g):
                dve.wait_ge(std_ready, g + 1)
                if g >= 2:
                    dve.wait_ge(rows_ready, U * (g - 1))
                dve.reciprocal(rstd[:, g % 2], std[:, g % 2]).then_inc(rstd_ready, 1)
                dve.wait_ge(rstd_ready, g + 1)
                dve.scalar_tensor_tensor(shift[:, g % 2], mean_var[:, g % 2, :, 0], -1.0, rstd[:, g % 2],
                                         ALU.mult, ALU.mult).then_inc(shift_ready, 1)

            for g in range(G):
                dve.wait_ge(x_hi_ready, g + 1)
                dve.tensor_tensor(x_lo[:, g], acc[:, g].rearrange("p (u c) -> p u c", u=U),
                                  x_hi[:, g].bitcast(F32), ALU.subtract).then_inc(x_lo_ready, 1)
                for n in range(g * U, (g + 1) * U):
                    dve.wait_ge(a_hi_ready, n + 1)
                    dve.tensor_tensor(lo[:, first_buffer(n)], adj_sb[:, g, n % U], hi[:, first_buffer(n)].bitcast(F32),
                                      ALU.subtract).then_inc(a_lo_ready_dve, 1)
                dve.wait_ge(x_transposed, g + 1)
                dve.wait_ge(x_lo_ready, g + 1)
                dve.tensor_copy(acc[:, g], at_ps[:, g % U]).then_inc(acc_written, 1)
                if g == 0:
                    dve.wait_ge(coef_transposed, 1)
                    dve.tensor_copy(coef[:], o_ps[:, 0, 0:KT]).then_inc(coef_ready, 1)
            for n in range(G * U, PROLOGUE):
                dve.wait_ge(a_hi_ready, n + 1)
                dve.tensor_tensor(lo[:, first_buffer(n)], adj_sb[:, n // U, n % U], hi[:, first_buffer(n)].bitcast(F32),
                                  ALU.subtract).then_inc(a_lo_ready_dve, 1)
            dve.wait_ge(coef_ready, 1)
            step(G)
            split_low_transposed(0)
            with dve.Fori(0, TURNS) as turn:
                for i in range(LAG, LAG + SLOTS):
                    step(i, turn)
            for i in range(LAG + LOOPED, GROUPS + LAG):
                step(i)
            shift_and_scale(G - 2)
            statistics(G - 1)
            shift_and_scale(G - 1)

        @block.tensor
        def _(pe):
            pe.wait_ge(ident_ready, 1)

            def transpose_tiles(m):
                for u in range(U):
                    last = pe.transpose(at_ps[:, m % U, u * P:(u + 1) * P],
                                        adj_sb[:, m // U % SLOTS, u, m % U * P:(m % U + 1) * P], ident[:])
                last.then_inc(at_transposed, 1)

            def first_product(n, turn=0):
                i, y = n // U, y_ps[:, n // U // G % 2]
                g, u = i % G, n % U
                first, end = g == 0 and u == 0, g == G - 1 and u == U - 1
                pe.wait_ge(a_hi_ready, turn * (SLOTS * U) + (n + 1))
                if first and i // G >= 2:
                    pe.wait_ge(s_scaled, turn * 2 + (i // G - 1))
                pe.matmul(y, x_hi[:, g, u], hi[:, first_buffer(n)], start=first, stop=False)
                pe.matmul(y, x_lo[:, g, u], hi[:, first_buffer(n)], start=False, stop=False)
                if n < PROLOGUE:
                    pe.wait_ge(a_lo_ready_dve, n + 1)
                else:
                    pe.wait_ge(a_lo_ready_pool, turn * (SLOTS * U) + (n + 1 - PROLOGUE))
                pe.matmul(y, x_hi[:, g, u], lo[:, first_buffer(n)], start=False, stop=end).then_inc(first_done, 1)

            def second_product(m, turn=0):
                j, k, o = m // U, m % U, o_ps[:, m // U % 2]
                s = j // G % 2
                if k == 0:
                    if j % G == 0:
                        pe.wait_ge(s_ready, turn * 2 + (j // G + 1))
                    pe.wait_ge(acc_written, turn * SLOTS + (G + j - 1))
                pe.wait_ge(at_hi_ready, turn * (SLOTS * U) + (m + 1))
                pe.matmul(o, s_hi[:, s, k], hi[:, second_buffer(m)], start=k == 0, stop=False)
                pe.matmul(o, s_lo[:, s, k], hi[:, second_buffer(m)], start=False, stop=False)
                pe.wait_ge(at_lo_ready, turn * (SLOTS * U) + (m + 1))
                pe.matmul(o, s_hi[:, s, k], lo[:, second_buffer(m)], start=False, stop=k == U - 1).then_inc(second_done, 1)

            def transpose_y(b, turn=0):
                pe.wait_ge(y_copied, turn * 2 + (b + 1))
                for u in range(U):
                    last = pe.transpose(y_ps[:, b % 2, u * C:(u + 1) * C], y_sb[:, u * P:(u + 1) * P], ident[:])
                last.then_inc(y_transposed, 1)

            def step(i, turn=0):
                j = i - LAG
                for u in range(U):
                    m = j * U + u
                    if m == TAIL:
                        transpose_tiles(m + 1)
                        transpose_tiles(m + 2)
                    if j >= 0 and m + transposes_ahead(m) < GROUPS * U:
                        transpose_tiles(m + transposes_ahead(m))
                    if i < GROUPS:
                        first_product(i * U + u, turn)
                    if starts_block(i) and u == 1:
                        transpose_y(i // G - 1, turn)
                    if j >= 0:
                        second_product(m, turn)
                    if u == 1 and finished(i) >= 0:
                        transpose_rows(finished(i))

            def transpose_rows(g):
                pe.wait_ge(acc_written, G + GROUPS - G + g + 1)
                if g >= 2:
                    pe.wait_ge(rows_ready, U * (g - 1))
                for u in range(U):
                    last = pe.transpose(y_ps[:, g % 2, u * C:(u + 1) * C], acc[:, g, u * P:(u + 1) * P], ident[:])
                last.then_inc(rows_transposed, 1)

            for g in range(G):
                pe.wait_ge(x_loaded[g], 16)
                if g >= U:
                    pe.wait_ge(acc_written, g - U + 1)
                for u in range(U):
                    last = pe.transpose(at_ps[:, g % U, u * P:(u + 1) * P], acc[:, g, u * C:(u + 1) * C], ident[:])
                last.then_inc(x_transposed, 1)
                if g == 0:
                    pe.wait_ge(coef_rows_ready, 1)
                    pe.transpose(o_ps[:, 0, 0:KT], coef_rows[:], ident[0:KT, 0:KT]).then_inc(coef_transposed, 1)
                pe.wait_ge(x_lo_ready, g + 1)
                step(g)
            step(G)
            pe.wait_ge(acc_written, U + 1)
            transpose_tiles(0)
            with pe.Fori(0, TURNS) as turn:
                for i in range(LAG, LAG + SLOTS):
                    step(i, turn)
            for i in range(LAG + LOOPED, GROUPS + LAG):
                step(i)
            transpose_rows(G - 1)


def kernel(x, adj, L0_gnn_evals, L0_gnn_t):
    import numpy as np
    from concourse import bacc
    from concourse.bass_utils import run_bass_kernel_spmd

    nc = bacc.Bacc("TRN2", target_bir_lowering=False, num_devices=1)
    given = {"x": x, "adj": adj, "evals": L0_gnn_evals, "t": L0_gnn_t}
    arrays = {name: np.ascontiguousarray(a) for name, a in given.items()}
    ins = [nc.dram_tensor(name, a.shape, mybir.dt.from_np(a.dtype), kind="ExternalInput").ap()
           for name, a in arrays.items()]
    out = nc.dram_tensor("out", arrays["x"].shape, F32, kind="ExternalOutput").ap()
    heat_layernorm(nc, *ins, out)
    return run_bass_kernel_spmd(nc, [arrays], core_ids=[0]).results[0]["out"]
```

```python
from contextlib import ExitStack

import concourse.bass as bass
from concourse import mybir

F32 = mybir.dt.float32
F32R = mybir.dt.float32r
ALU = mybir.AluOpType
ACT = mybir.ActivationFunctionType

P = 128
Q = 32
W = 512
U = W // P
BUFFERS = 4
KEPT = 8
PASSING = 2
TURN = 16
EPS = 1e-5
T_MIN = 1e-8


def heat_layernorm(nc: bass.Bass, x: bass.AP, adj: bass.AP, evals: bass.AP, t: bass.AP, out: bass.AP):
    N, C = x.shape
    G = N // W
    B = N // W
    GROUPS = B * G
    TILES = GROUPS * U
    LAG = G + 1
    KT = N // P
    TURNS = (GROUPS - LAG) // TURN
    TT = TURN * U
    LEAD = LAG * U
    TAIL = TILES - LEAD
    assert C == P and N % W == 0 and TURN == 2 * G == 2 * KEPT and B % 2 == 0 and LAG % 2 == 1

    def rows(a, g):
        if g % 2 == 0:
            return a.rearrange("(g p u) c -> g p u c", p=P, u=U)[g]
        return a.rearrange("(g u p) c -> g p u c", p=P, u=U)[g]

    adj_by_quadrant = adj.rearrange("(g m r) k -> g r m k", r=Q, m=W // Q)

    with ExitStack() as ctx:
        def sb(name, shape, dt=F32):
            return ctx.enter_context(nc.sbuf_tensor(name, shape, dt))

        def sem(name):
            return ctx.enter_context(nc.semaphore(name))

        kept = sb("kept", [P, KEPT, U, W])
        passing = sb("passing", [P, PASSING, U, W])
        again = sb("again", [P, PASSING, W // Q, P])
        x_hi = sb("x_hi", [P, G, U, C], F32R)
        x_lo = sb("x_lo", [P, G, U, C], F32R)
        acc = sb("acc", [P, G, W])
        a_hi = sb("a_hi", [P, BUFFERS, W], F32R)
        a_lo = sb("a_lo", [P, BUFFERS, W], F32R)
        at_hi = sb("at_hi", [P, BUFFERS, W], F32R)
        at_lo = sb("at_lo", [P, BUFFERS, W], F32R)
        y_sb = sb("y_sb", [P, 2, W])
        s_hi = sb("s_hi", [P, 2, 2, U, C], F32R)
        s_lo = sb("s_lo", [P, 2, 2, U, C], F32R)
        ident = sb("ident", [P, P])
        evals_sb = sb("evals_sb", [KT, 2, P])
        t_sb = sb("t_sb", [KT, 1])
        neg_t = sb("neg_t", [KT, 1])
        coef_rows = sb("coef_rows", [KT, 2, P])
        coef = sb("coef", [P, 2, KT])
        eps_sb = sb("eps_sb", [P, 1])
        stats = sb("stats", [P, U, 6])
        mean_var = sb("mean_var", [P, 2, U, 2])
        std = sb("std", [P, 2, U])
        rstd = sb("rstd", [P, 2, U])
        shift = sb("shift", [P, 2, U])

        y_ps = ctx.enter_context(nc.psum_tensor("y_ps", [P, 2, W], F32))
        o_ps = ctx.enter_context(nc.psum_tensor("o_ps", [P, 2, W], F32))
        at_ps = ctx.enter_context(nc.psum_tensor("at_ps", [P, U, W], F32))

        x_loaded = [sem(f"x_loaded{g}") for g in range(G)]
        kept_loaded = [sem(f"kept_loaded{k}") for k in range(KEPT)]
        passing_loaded = [sem(f"passing_loaded{k}") for k in range(PASSING)]
        again_loaded = [sem(f"again_loaded{k}") for k in range(PASSING)]
        spectrum_loaded = sem("spectrum_loaded")
        out_stored = sem("out_stored")
        ident_zeroed = sem("ident_zeroed")
        ident_ready = sem("ident_ready")
        t_ready = sem("t_ready")
        eps_ready = sem("eps_ready")
        coef_rows_ready = sem("coef_rows_ready")
        coef_transposed = sem("coef_transposed")
        coef_ready = sem("coef_ready")
        x_hi_ready = sem("x_hi_ready")
        x_lo_ready = sem("x_lo_ready")
        x_transposed = sem("x_transposed")
        a_hi_ready = sem("a_hi_ready")
        a_lo_ready_dve = sem("a_lo_ready_dve")
        a_lo_ready_pool = sem("a_lo_ready_pool")
        first_done = sem("first_done")
        at_transposed = sem("at_transposed")
        at_turned = sem("at_turned")
        at_hi_ready = sem("at_hi_ready")
        at_lo_ready_dve = sem("at_lo_ready_dve")
        at_lo_ready_pool = sem("at_lo_ready_pool")
        second_done = sem("second_done")
        acc_written = sem("acc_written")
        y_copied = sem("y_copied")
        y_transposed = sem("y_transposed")
        s_scaled = sem("s_scaled")
        s_hi_ready = sem("s_hi_ready")
        s_ready = sem("s_ready")
        rows_transposed = sem("rows_transposed")
        stats_ready = sem("stats_ready")
        mean_var_ready = sem("mean_var_ready")
        std_ready = sem("std_ready")
        rstd_ready = sem("rstd_ready")
        shift_ready = sem("shift_ready")
        rows_ready = sem("rows_ready")

        def adj_tile(n):
            i = n // U
            return kept[:, i // 2 % KEPT, n % U] if i % 2 == 0 else passing[:, i // 2 % PASSING, n % U]

        def hi_order(j):
            if j * U <= TAIL:
                return [[j * U + u] for u in range(U)]
            return [[j * U + u, (j + 1) * U + u] if j % 2 == 0 else [] for u in range(U)]

        def hi_count(m):
            if m < TAIL + U:
                return m + 1
            return m // (2 * U) * (2 * U) + 2 * (m % U) + 1 + odd(m)

        def own(m):
            return m // U // 2 * U + m % U + 1

        def odd(m):
            return m // U % 2 == 1

        def on_pool(m):
            return m >= TAIL and odd(m)

        def pool_count(m):
            return sum(on_pool(k) for k in range(TAIL, m + 1))

        def turned_tile(m):
            return passing[:, (m // U // 2 + 1) % PASSING, m % U]

        def at_tile(m):
            return turned_tile(m) if on_pool(m) else at_ps[:, m % U]

        def at_hi_tile(m):
            return (a_hi if m >= TAIL and (m - TAIL) // BUFFERS % 2 == 0 else at_hi)[:, m % BUFFERS]

        def at_lo_tile(m):
            return (a_lo if m >= TAIL and (m - TAIL) // BUFFERS % 2 == 0 else at_lo)[:, m % BUFFERS]

        def finished(i):
            return i - LAG - 1 - (GROUPS - G)

        def s_made(i):
            return [(i // G - 1, i % G)] if i % G < 2 and G <= i <= GROUPS + 1 else []

        out_rows = [kept[:, 0:2].rearrange("p k u w -> p (k u) w")[:, g] for g in range(G)]

        block = ctx.enter_context(nc.Block())


        @block.sync
        def _(sp):
            def load_kept(i, turn=0):
                sp.dma_start(kept[:, i // 2 % KEPT], rows(adj, i % G)[:, :, bass.ts(turn * 2 + i // G, W)]
                             ).then_inc(kept_loaded[i // 2 % KEPT], 16)

            def load_passing(i, turn=0):
                sp.dma_start(passing[:, i // 2 % PASSING], rows(adj, i % G)[:, :, bass.ts(turn * 2 + i // G, W)]
                             ).then_inc(passing_loaded[i // 2 % PASSING], 16)

            def load_again(j, turn=0):
                for b in range(U):
                    columns = bass.ds(turn * (2 * W) + (j // G * W + b * P), P)
                    sp.dma_start(again[b * Q:(b + 1) * Q, j // 2 % PASSING], adj_by_quadrant[j % G, :, :, columns]
                                 ).then_inc(again_loaded[j // 2 % PASSING], 16)

            def step(i, turn=0):
                j = i - LAG
                if i % 2 == 1:
                    if 0 <= j and i + 7 < GROUPS:
                        sp.wait_ge(at_transposed, turn * (TT // 2) + own(j * U + U - 1))
                        load_kept(i + 7, turn)
                    if i + 4 < GROUPS:
                        sp.wait_ge(first_done, turn * TT + (i + 1) * U)
                        load_passing(i + 4, turn)
                elif 0 <= j and j + 4 < GROUPS:
                    sp.wait_ge(at_turned, turn * (TT // 2) + own(j * U + U - 1))
                    load_again(j + 4, turn)

            for i in range(LAG + 6):
                if i < G:
                    sp.dma_start(acc[:, i].rearrange("p (u c) -> p u c", u=U), rows(x, i)).then_inc(x_loaded[i], 16)
                if i % 2 == 0:
                    load_kept(i)
                elif i < 4:
                    load_passing(i)
                elif i <= LAG + 2:
                    step(i - 4)
                if i == LAG + 1:
                    load_again(1)
                if i == LAG + 3:
                    load_again(3)
            with sp.Fori(0, TURNS) as turn:
                for i in range(LAG, LAG + TURN):
                    step(i, turn)
            for i in range(LAG + TURNS * TURN, GROUPS + LAG):
                step(i)
            for g in range(G):
                sp.wait_ge(rows_ready, U * (g + 1))
                sp.dma_start(rows(out, g), out_rows[g].rearrange("p (u c) -> p u c", u=U)).then_inc(out_stored, 16)
            sp.wait_ge(out_stored, 16 * G)

        @block.gpsimd
        def _(pool):
            pool.memset(ident[:], 0.0).then_inc(ident_zeroed, 1)
            pool.wait_ge(ident_zeroed, 1)
            pool.affine_select(out=ident[:], in_=ident[:], compare_op=ALU.not_equal, fill=1.0, base=0,
                               pattern=[[-1, P]], channel_multiplier=1).then_inc(ident_ready, 1)
            pool.dma_start(evals_sb[:, 0], evals.rearrange("(k p) -> k p", p=P)).then_inc(spectrum_loaded, 16)
            for b in range(B):
                pool.dma_start(evals_sb[b * U:(b + 1) * U, 1].rearrange("k (b c) -> k b c", c=Q),
                              evals[b * W:(b + 1) * W].rearrange("(b k c) -> k b c", k=U, c=Q)
                              ).then_inc(spectrum_loaded, 16)
            pool.dma_start(t_sb[:], t.rearrange("(a b) -> a b", a=1).to_broadcast([KT, 1])).then_inc(spectrum_loaded, 16)

            def split_low(n, turn=0):
                pool.wait_ge(a_hi_ready, turn * TT + (n + 1))
                pool.tensor_tensor(a_lo[:, n % BUFFERS], adj_tile(n), a_hi[:, n % BUFFERS].bitcast(F32),
                                   ALU.subtract).then_inc(a_lo_ready_pool, 1)

            with pool.Fori(0, TURNS) as turn:
                for n in range(LEAD, LEAD + TT):
                    split_low(n, turn)
            for n in range(LEAD + TURNS * TT, TILES):
                split_low(n)
            for m in range(TAIL, TILES):
                if on_pool(m):
                    pool.wait_ge(at_hi_ready, hi_count(m))
                    pool.tensor_tensor(at_lo_tile(m), turned_tile(m), at_hi_tile(m).bitcast(F32),
                                       ALU.subtract).then_inc(at_lo_ready_pool, 1)

        @block.scalar
        def _(act):
            def split_high(n, turn=0):
                i = n // U
                if n % U == 0 and i % 2 == 0:
                    act.wait_ge(kept_loaded[i // 2 % KEPT], turn * 16 + 16 * (i // 2 // KEPT + 1))
                if n % U == 0 and i % 2 == 1:
                    act.wait_ge(passing_loaded[i // 2 % PASSING],
                                turn * (16 * TURN // 2 // PASSING) + 16 * (i // 2 // PASSING + 1))
                if n >= BUFFERS:
                    act.wait_ge(first_done, turn * TT + (n + 1 - BUFFERS))
                act.activation(a_hi[:, n % BUFFERS], adj_tile(n), ACT.Copy).then_inc(a_hi_ready, 1)

            def split_high_transposed(m, turn=0):
                if odd(m):
                    act.wait_ge(at_turned, turn * (TT // 2) + own(m))
                    act.wait_ge(second_done, turn * TT + (m + 1 - (2 * BUFFERS if m >= TAIL else BUFFERS)))
                else:
                    act.wait_ge(at_transposed, turn * (TT // 2) + own(m))
                if TAIL <= m < TAIL + BUFFERS:
                    act.wait_ge(first_done, m + 1 - TAIL + TILES - BUFFERS)
                act.activation(at_hi_tile(m), at_tile(m), ACT.Copy).then_inc(at_hi_ready, 1)

            def copy_y(b, turn=0):
                act.wait_ge(first_done, turn * TT + G * U * (b + 1))
                if b >= 1:
                    act.wait_ge(s_ready, turn * 4 + 2 * b)
                act.activation(y_sb[:, 0], y_ps[:, b % 2], ACT.Copy).then_inc(y_copied, 1)
                act.activation(y_sb[:, 1].rearrange("p (k b c) -> p k b c", k=U, c=Q),
                               y_ps[:, b % 2].rearrange("p (b k c) -> p k b c", k=U, c=Q), ACT.Copy).then_inc(y_copied, 1)

            def split_s_high(b, order, turn=0):
                act.wait_ge(s_scaled, turn * 4 + (2 * b + order + 1))
                if b >= 2:
                    act.wait_ge(second_done, turn * TT + G * U * (b - 1))
                act.activation(s_hi[:, b % 2, order], y_sb[:, order].rearrange("p (u c) -> p u c", u=U), ACT.Copy).then_inc(s_hi_ready, 1)

            def deviation(g):
                act.wait_ge(mean_var_ready, g + 1)
                if g >= 2:
                    act.wait_ge(rstd_ready, g - 1)
                act.activation(std[:, g % 2], mean_var[:, g % 2, :, 1], ACT.Sqrt, bias=eps_sb[:]).then_inc(std_ready, 1)

            def normalise(g, u):
                act.wait_ge(shift_ready, g + 1)
                act.activation(out_rows[g][:, u * C:(u + 1) * C], y_ps[:, g % 2, u * C:(u + 1) * C], ACT.Identity,
                               scale=rstd[:, g % 2, u:u + 1], bias=shift[:, g % 2, u:u + 1]).then_inc(rows_ready, 1)

            def step(i, turn=0):
                j = i - LAG
                for u in range(U):
                    if i < GROUPS:
                        split_high(i * U + u, turn)
                    for b, order in s_made(i):
                        if order == 0 and u == 2:
                            copy_y(b, turn)
                    if j >= 0:
                        for m in hi_order(j)[u]:
                            split_high_transposed(m, turn)
                    for b, order in s_made(i - 1):
                        if u == 1:
                            split_s_high(b, order, turn)
                    if u == 1 and finished(i) >= 1:
                        deviation(finished(i) - 1)
                    if u == 3 and finished(i) >= 1:
                        normalise(finished(i) - 1, 0)
                    if u < 3 and finished(i) >= 2:
                        normalise(finished(i) - 2, u + 1)

            for g in range(G):
                act.wait_ge(x_loaded[g], 16)
                act.activation(x_hi[:, g], acc[:, g].rearrange("p (u c) -> p u c", u=U), ACT.Copy).then_inc(x_hi_ready, 1)
                step(g)
                act.wait_ge(x_transposed, g + 1)
                act.wait_ge(x_lo_ready, g + 1)
                act.activation(acc[:, g], at_ps[:, g % U], ACT.Copy).then_inc(acc_written, 1)
            act.wait_ge(spectrum_loaded, 16 * (B + 2))
            act.wait_ge(t_ready, 1)
            act.activation(coef_rows[:], evals_sb[:], ACT.Exp, scale=neg_t[:]).then_inc(coef_rows_ready, 1)
            step(G)
            with act.Fori(0, TURNS) as turn:
                for i in range(LAG, LAG + TURN):
                    step(i, turn)
            act.wait_ge(eps_ready, 1)
            for i in range(LAG + TURNS * TURN, GROUPS + LAG):
                step(i)
            for u in range(1, U):
                normalise(G - 3, u)
            for g in (G - 2, G - 1):
                deviation(g)
                for u in range(U):
                    normalise(g, u)

        @block.vector
        def _(dve):
            dve.memset(eps_sb[:], EPS).then_inc(eps_ready, 1)

            def split_low(n):
                dve.wait_ge(a_hi_ready, n + 1)
                dve.tensor_tensor(a_lo[:, n % BUFFERS], adj_tile(n), a_hi[:, n % BUFFERS].bitcast(F32),
                                  ALU.subtract).then_inc(a_lo_ready_dve, 1)

            def turn_tile(m, turn=0):
                j = m // U
                if m % U == 0:
                    dve.wait_ge(again_loaded[j // 2 % PASSING],
                                turn * (16 * U * TURN // 2 // PASSING) + 16 * U * (j // 2 // PASSING + 1))
                if not on_pool(m):
                    dve.wait_ge(at_lo_ready_dve, turn * TT + (m - U + 1))
                elif m < TAIL + 4 * U:
                    dve.wait_ge(first_done, TILES - (2 * U if m < TAIL + 2 * U else 0))
                else:
                    dve.wait_ge(at_lo_ready_pool, pool_count(m - 4 * U))
                k = m % U
                dve.transpose(at_tile(m).rearrange("p (m r) -> p m r", r=Q),
                              again[:, j // 2 % PASSING, :, k * Q:(k + 1) * Q]).then_inc(at_turned, 1)

            def split_low_transposed(m, turn=0):
                dve.wait_ge(at_hi_ready, turn * TT + hi_count(m))
                dve.tensor_tensor(at_lo_tile(m), at_tile(m),
                                  at_hi_tile(m).bitcast(F32), ALU.subtract).then_inc(at_lo_ready_dve, 1)

            def accumulate(j, turn=0):
                dve.wait_ge(second_done, turn * TT + U * (j + 1))
                dve.tensor_tensor(acc[:, j % G], o_ps[:, j % 2], acc[:, j % G], ALU.add).then_inc(acc_written, 1)

            def scale_s(b, order, turn=0):
                dve.wait_ge(y_transposed, turn * 4 + (2 * b + order + 1))
                c = coef[:, order, bass.ds(turn * (2 * U) + b * U, U)].unsqueeze(2).to_broadcast([P, U, C])
                dve.tensor_tensor(y_sb[:, order].rearrange("p (u c) -> p u c", u=U),
                                  y_ps[:, b % 2].rearrange("p (u c) -> p u c", u=U), c, ALU.mult).then_inc(s_scaled, 1)

            def split_s_low(b, order, turn=0):
                dve.wait_ge(s_hi_ready, turn * 4 + (2 * b + order + 1))
                dve.tensor_tensor(s_lo[:, b % 2, order], y_sb[:, order].rearrange("p (u c) -> p u c", u=U),
                                  s_hi[:, b % 2, order].bitcast(F32), ALU.subtract).then_inc(s_ready, 1)

            def statistics(g):
                dve.wait_ge(rows_transposed, g + 1)
                for u in range(U):
                    dve.bn_stats(stats[:, u], y_ps[:, g % 2, u * C:(u + 1) * C]).then_inc(stats_ready, 1)
                dve.wait_ge(stats_ready, U * (g + 1))
                if g >= 2:
                    dve.wait_ge(std_ready, g - 1)
                for u in range(U):
                    last = dve.bn_aggr(mean_var[:, g % 2, u], stats[:, u])
                last.then_inc(mean_var_ready, 1)

            def shift_and_scale(g):
                dve.wait_ge(std_ready, g + 1)
                if g >= 2:
                    dve.wait_ge(rows_ready, U * (g - 1))
                dve.reciprocal(rstd[:, g % 2], std[:, g % 2]).then_inc(rstd_ready, 1)
                dve.wait_ge(rstd_ready, g + 1)
                dve.scalar_tensor_tensor(shift[:, g % 2], mean_var[:, g % 2, :, 0], -1.0, rstd[:, g % 2],
                                         ALU.mult, ALU.mult).then_inc(shift_ready, 1)

            def tile_step(i, u, turn=0):
                j = i - LAG
                m = j * U + u
                for b, order in s_made(i):
                    if u == 3:
                        scale_s(b, order, turn)
                for b, order in s_made(i - 1):
                    if u == 0:
                        split_s_low(b, order, turn)
                if u == 0 and finished(i) >= 1:
                    shift_and_scale(finished(i) - 1)
                if u == 3 and finished(i) >= 0:
                    statistics(finished(i))
                if j >= 0 and m + 2 < TILES and not on_pool(m + 2):
                    split_low_transposed(m + 2, turn)
                ahead = 4 if m + 4 < TAIL + U else 7
                if j >= 0 and m + ahead < TILES and odd(m + ahead):
                    turn_tile(m + ahead, turn)

            def step(i, turn=0):
                for u in range(1, U):
                    tile_step(i, u, turn)
                tile_step(i + 1, 0, turn)
                if i >= LAG:
                    accumulate(i - LAG, turn)

            for g in range(G):
                dve.wait_ge(x_hi_ready, g + 1)
                dve.tensor_tensor(x_lo[:, g], acc[:, g].rearrange("p (u c) -> p u c", u=U),
                                  x_hi[:, g].bitcast(F32), ALU.subtract).then_inc(x_lo_ready, 1)
                for n in range(g * U, (g + 1) * U):
                    split_low(n)
            dve.wait_ge(spectrum_loaded, 16 * (B + 2))
            dve.tensor_scalar(neg_t[:], t_sb[:], T_MIN, -1.0, ALU.max, ALU.mult).then_inc(t_ready, 1)
            for n in range(G * U, LEAD):
                split_low(n)
            dve.wait_ge(coef_transposed, 1)
            dve.tensor_copy(coef[:].rearrange("p o k -> p (o k)"), o_ps[:, 0, 0:2 * KT]).then_inc(coef_ready, 1)
            dve.wait_ge(coef_ready, 1)
            for u in range(U):
                tile_step(G, u)
            split_low_transposed(0)
            split_low_transposed(1)
            tile_step(LAG, 0)
            with dve.Fori(0, TURNS) as turn:
                for i in range(LAG, LAG + TURN):
                    step(i, turn)
            for i in range(LAG + TURNS * TURN, GROUPS + LAG):
                step(i)
            statistics(G - 1)
            shift_and_scale(G - 1)

        @block.tensor
        def _(pe):
            pe.wait_ge(ident_ready, 1)

            def transpose_tiles(m):
                for u in range(U):
                    last = pe.transpose(at_ps[:, m % U, u * P:(u + 1) * P],
                                        kept[:, m // U // 2 % KEPT, u, m % U * P:(m % U + 1) * P], ident[:])
                last.then_inc(at_transposed, 1)

            def first_product(n, turn=0):
                i, y = n // U, y_ps[:, n // U // G % 2]
                g, u = i % G, n % U
                first, end = g == 0 and u == 0, g == G - 1 and u == U - 1
                hi, lo = a_hi[:, n % BUFFERS], a_lo[:, n % BUFFERS]
                pe.wait_ge(a_hi_ready, turn * TT + (n + 1))
                if first and i // G >= 2:
                    pe.wait_ge(s_scaled, turn * 4 + 2 * (i // G - 1))
                pe.matmul(y, x_hi[:, g, u], hi, start=first, stop=False)
                pe.matmul(y, x_lo[:, g, u], hi, start=False, stop=False)
                if n < LEAD:
                    pe.wait_ge(a_lo_ready_dve, n + 1)
                else:
                    pe.wait_ge(a_lo_ready_pool, turn * TT + (n + 1 - LEAD))
                pe.matmul(y, x_hi[:, g, u], lo, start=False, stop=end).then_inc(first_done, 1)

            def second_product(m, turn=0):
                j, k, o = m // U, m % U, o_ps[:, m // U % 2]
                s_h, s_l = s_hi[:, j // G % 2, j % 2, k], s_lo[:, j // G % 2, j % 2, k]
                hi, lo = at_hi_tile(m), at_lo_tile(m)
                if k == 0:
                    if j % G < 2:
                        pe.wait_ge(s_ready, turn * 4 + (2 * (j // G) + j % G + 1))
                    pe.wait_ge(acc_written, turn * TURN + (G + j - 1))
                pe.wait_ge(at_hi_ready, turn * TT + hi_count(m))
                pe.matmul(o, s_h, hi, start=k == 0, stop=False)
                pe.matmul(o, s_l, hi, start=False, stop=False)
                if on_pool(m):
                    pe.wait_ge(at_lo_ready_pool, pool_count(m))
                elif m >= TAIL:
                    pe.wait_ge(at_lo_ready_dve, m + 1 - pool_count(m))
                else:
                    pe.wait_ge(at_lo_ready_dve, turn * TT + (m + 1))
                pe.matmul(o, s_h, lo, start=False, stop=k == U - 1).then_inc(second_done, 1)

            def transpose_y(b, order, turn=0):
                pe.wait_ge(y_copied, turn * 4 + 2 * (b + 1))
                if order == 1:
                    pe.wait_ge(s_scaled, turn * 4 + (2 * b + 1))
                for k in range(U):
                    last = pe.transpose(y_ps[:, b % 2, k * C:(k + 1) * C], y_sb[:, order, k * P:(k + 1) * P], ident[:])
                last.then_inc(y_transposed, 1)

            def transpose_rows(g):
                pe.wait_ge(acc_written, GROUPS + g + 1)
                if g >= 2:
                    pe.wait_ge(rows_ready, U * (g - 1))
                for u in range(U):
                    last = pe.transpose(y_ps[:, g % 2, u * C:(u + 1) * C], acc[:, g, u * P:(u + 1) * P], ident[:])
                last.then_inc(rows_transposed, 1)

            def step(i, turn=0):
                j = i - LAG
                for u in range(U):
                    m = j * U + u
                    if j >= 0 and m + 3 < TILES and not odd(m + 3):
                        transpose_tiles(m + 3)
                    if i < GROUPS:
                        first_product(i * U + u, turn)
                    for b, order in s_made(i):
                        if u == 1:
                            transpose_y(b, order, turn)
                    if j >= 0:
                        second_product(m, turn)
                    if u == 1 and finished(i) >= 0:
                        transpose_rows(finished(i))

            for g in range(G):
                pe.wait_ge(x_loaded[g], 16)
                if g >= U:
                    pe.wait_ge(acc_written, g - U + 1)
                for u in range(U):
                    last = pe.transpose(at_ps[:, g % U, u * P:(u + 1) * P], acc[:, g, u * C:(u + 1) * C], ident[:])
                last.then_inc(x_transposed, 1)
                pe.wait_ge(x_lo_ready, g + 1)
                step(g)
            pe.wait_ge(coef_rows_ready, 1)
            for order in range(2):
                last = pe.transpose(o_ps[:, 0, order * KT:(order + 1) * KT], coef_rows[:, order],
                                    ident[0:KT, 0:KT])
            last.then_inc(coef_transposed, 1)
            step(G)
            pe.wait_ge(acc_written, G)
            for m in range(3):
                transpose_tiles(m)
            with pe.Fori(0, TURNS) as turn:
                for i in range(LAG, LAG + TURN):
                    step(i, turn)
            for i in range(LAG + TURNS * TURN, GROUPS + LAG):
                step(i)
            transpose_rows(G - 1)


def kernel(x, adj, L0_gnn_evals, L0_gnn_t):
    import numpy as np
    from concourse import bacc
    from concourse.bass_utils import run_bass_kernel_spmd

    nc = bacc.Bacc("TRN2", target_bir_lowering=False, num_devices=1)
    given = {"x": x, "adj": adj, "evals": L0_gnn_evals, "t": L0_gnn_t}
    arrays = {name: np.ascontiguousarray(a) for name, a in given.items()}
    ins = [nc.dram_tensor(name, a.shape, mybir.dt.from_np(a.dtype), kind="ExternalInput").ap()
           for name, a in arrays.items()]
    out = nc.dram_tensor("out", arrays["x"].shape, F32, kind="ExternalOutput").ap()
    heat_layernorm(nc, *ins, out)
    return run_bass_kernel_spmd(nc, [arrays], core_ids=[0]).results[0]["out"]
```

```python
from contextlib import ExitStack

import concourse.bass as bass
from concourse import mybir

F32 = mybir.dt.float32
F32R = mybir.dt.float32r
ALU = mybir.AluOpType
ACT = mybir.ActivationFunctionType

P = 128
Q = 32
W = 512
U = W // P
BUFFERS = 4
TURN = 16
TURNED = (1, 2, 4, 5, 6, 7, 9, 11, 13, 15)
KEPT = TURN - len(TURNED)
PASSING = 3
EPS = 1e-5
T_MIN = 1e-8


def heat_layernorm(nc: bass.Bass, x: bass.AP, adj: bass.AP, evals: bass.AP, t: bass.AP, out: bass.AP):
    N, C = x.shape
    G = N // W
    B = N // W
    GROUPS = B * G
    TILES = GROUPS * U
    LAG = G + 1
    KT = N // P
    TURNS = (GROUPS - LAG) // TURN
    TT = TURN * U
    LEAD = LAG * U
    TAIL = TILES - LEAD
    assert C == P and N % W == 0 and TURN == 2 * G and B % 2 == 0 and LAG % 2 == 1
    assert all(i % 2 == (i in TURNED) for i in (0, 1, *range(G, TURN)))

    def rows(a, g):
        return a.rearrange("(g u p) c -> g p u c", p=P, u=U)[g]

    def turned(i):
        return i % TURN in TURNED

    def rank(i):
        return sum(turned(k) == turned(i) for k in range(i))

    def slot(i):
        if not turned(i):
            return rank(i) % KEPT
        r = rank(i) % len(TURNED)
        return 1 if r == len(TURNED) - 1 and r % PASSING == 0 else r % PASSING

    def use(i):
        return sum(turned(k) == turned(i) and slot(k) == slot(i) for k in range(i + 1))

    def uses_in_turn(i):
        return sum(turned(k) == turned(i) and slot(k) == slot(i) for k in range(TURN))

    def next_in_slot(i):
        return next(k for k in range(i + 1, i + TURN + 1) if turned(k) == turned(i) and slot(k) == slot(i))

    adj_by_quadrant = adj.rearrange("(g m r) k -> g r m k", r=Q, m=W // Q)

    with ExitStack() as ctx:
        def sb(name, shape, dt=F32):
            return ctx.enter_context(nc.sbuf_tensor(name, shape, dt))

        def sem(name):
            return ctx.enter_context(nc.semaphore(name))

        kept = sb("kept", [P, KEPT, U, W])
        passing = sb("passing", [P, PASSING, U, W])
        again = sb("again", [P, PASSING, W // Q, P])
        x_hi = sb("x_hi", [P, G, U, C], F32R)
        x_lo = sb("x_lo", [P, G, U, C], F32R)
        acc = sb("acc", [P, G, W])
        a_hi = sb("a_hi", [P, BUFFERS, W], F32R)
        a_lo = sb("a_lo", [P, BUFFERS, W], F32R)
        at_hi = sb("at_hi", [P, BUFFERS, W], F32R)
        at_lo = sb("at_lo", [P, BUFFERS, W], F32R)
        y_sb = sb("y_sb", [P, 2, W])
        s_hi = sb("s_hi", [P, 2, 2, U, C], F32R)
        s_lo = sb("s_lo", [P, 2, 2, U, C], F32R)
        ident = sb("ident", [P, P])
        evals_sb = sb("evals_sb", [KT, 2, P])
        t_sb = sb("t_sb", [KT, 1])
        neg_t = sb("neg_t", [KT, 1])
        coef_rows = sb("coef_rows", [KT, 2, P])
        coef = sb("coef", [P, 2, KT])
        eps_sb = sb("eps_sb", [P, 1])
        stats = sb("stats", [P, U, 6])
        mean_var = sb("mean_var", [P, 2, U, 2])
        std = sb("std", [P, 2, U])
        rstd = sb("rstd", [P, 2, U])
        shift = sb("shift", [P, 2, U])

        y_ps = ctx.enter_context(nc.psum_tensor("y_ps", [P, 2, W], F32))
        o_ps = ctx.enter_context(nc.psum_tensor("o_ps", [P, 2, W], F32))
        at_ps = ctx.enter_context(nc.psum_tensor("at_ps", [P, U, W], F32))

        x_loaded = [sem(f"x_loaded{g}") for g in range(G)]
        kept_loaded = [sem(f"kept_loaded{k}") for k in range(KEPT)]
        passing_loaded = [sem(f"passing_loaded{k}") for k in range(PASSING)]
        again_loaded = [sem(f"again_loaded{k}") for k in range(PASSING)]
        spectrum_loaded = sem("spectrum_loaded")
        out_stored = sem("out_stored")
        ident_zeroed = sem("ident_zeroed")
        ident_ready = sem("ident_ready")
        t_ready = sem("t_ready")
        eps_ready = sem("eps_ready")
        coef_rows_ready = sem("coef_rows_ready")
        coef_transposed = sem("coef_transposed")
        coef_ready = sem("coef_ready")
        x_hi_ready = sem("x_hi_ready")
        x_lo_ready = sem("x_lo_ready")
        x_transposed = sem("x_transposed")
        a_hi_ready = sem("a_hi_ready")
        a_lo_ready_dve = sem("a_lo_ready_dve")
        a_lo_ready_pool = sem("a_lo_ready_pool")
        first_done = sem("first_done")
        at_transposed = sem("at_transposed")
        at_turned = sem("at_turned")
        at_hi_ready = sem("at_hi_ready")
        at_lo_ready_dve = sem("at_lo_ready_dve")
        at_lo_ready_pool = sem("at_lo_ready_pool")
        second_done = sem("second_done")
        acc_written = sem("acc_written")
        y_copied = sem("y_copied")
        y_transposed = sem("y_transposed")
        s_scaled = sem("s_scaled")
        s_hi_ready = sem("s_hi_ready")
        s_ready = sem("s_ready")
        rows_transposed = sem("rows_transposed")
        stats_ready = sem("stats_ready")
        mean_var_ready = sem("mean_var_ready")
        std_ready = sem("std_ready")
        rstd_ready = sem("rstd_ready")
        shift_ready = sem("shift_ready")
        rows_ready = sem("rows_ready")
        rows_ready_dve = sem("rows_ready_dve")

        def adj_tile(n):
            i = n // U
            return (passing if turned(i) else kept)[:, slot(i), n % U]

        def hi_order(j):
            if j * U <= TAIL:
                return [[j * U + u] for u in range(U)]
            return [[j * U + u, (j + 1) * U + u] if j % 2 == 0 else [] for u in range(U)]

        def hi_count(m):
            if m < TAIL + U:
                return m + 1
            return m // (2 * U) * (2 * U) + 2 * (m % U) + 1 + turned(m // U)

        def own(m):
            return rank(m // U) * U + m % U + 1

        def own_in_turn(m):
            return U * (len(TURNED) if turned(m // U) else KEPT)

        def on_pool(m):
            return m >= TAIL and turned(m // U)

        def pool_count(m):
            return sum(on_pool(k) for k in range(TAIL, m + 1))

        def turned_tile(m):
            return passing[:, (m // U // 2 + 1) % 2, m % U]

        def at_tile(m):
            return turned_tile(m) if on_pool(m) else at_ps[:, m % U]

        def at_hi_tile(m):
            return (a_hi if m >= TAIL and (m - TAIL) // BUFFERS % 2 == 0 else at_hi)[:, m % BUFFERS]

        def at_lo_tile(m):
            return (a_lo if m >= TAIL and (m - TAIL) // BUFFERS % 2 == 0 else at_lo)[:, m % BUFFERS]

        def finished(i):
            return i - LAG - 1 - (GROUPS - G)

        def s_made(i):
            return [(i // G - 1, i % G)] if i % G < 2 and G <= i <= GROUPS + 1 else []

        def rows_ps(g, u):
            bank = at_ps[:, 0] if g == G - 1 and u >= U // 2 else y_ps[:, g % 2]
            return bank[:, u * C:(u + 1) * C]

        out_rows = [kept[:, 0:2].rearrange("p k u w -> p (k u) w")[:, g] for g in range(G)]

        block = ctx.enter_context(nc.Block())


        @block.sync
        def _(sp):
            def load(i, turn=0):
                place, loaded = (passing, passing_loaded) if turned(i) else (kept, kept_loaded)
                sp.dma_start(place[:, slot(i)], rows(adj, i % G)[:, :, bass.ts(turn * 2 + i // G, W)]
                             ).then_inc(loaded[slot(i)], 16)

            def load_again(j, turn=0):
                for b in range(U):
                    columns = bass.ds(turn * (2 * W) + (j // G * W + b * P), P)
                    sp.dma_start(again[b * Q:(b + 1) * Q, slot(j)], adj_by_quadrant[j % G, :, :, columns]
                                 ).then_inc(again_loaded[slot(j)], 16)

            def step(i, turn=0):
                j = i - LAG
                last = j * U + U - 1
                if j >= 0 and next_in_slot(j) < GROUPS:
                    if turned(j):
                        sp.wait_ge(at_turned, turn * own_in_turn(last) + own(last))
                        load_again(next_in_slot(j), turn)
                    else:
                        sp.wait_ge(at_transposed, turn * own_in_turn(last) + own(last))
                        load(next_in_slot(j), turn)
                if turned(i) and next_in_slot(i) < GROUPS:
                    sp.wait_ge(first_done, turn * TT + (i + 1) * U)
                    load(next_in_slot(i), turn)

            first_turned = TURNED[:PASSING]
            for i in range(TURN):
                if i < G:
                    sp.dma_start(acc[:, i].rearrange("p (u c) -> p u c", u=U), rows(x, i)).then_inc(x_loaded[i], 16)
                if not turned(i) or i in first_turned:
                    load(i)
                else:
                    before = next(k for k in range(i) if turned(k) and next_in_slot(k) == i)
                    if before < LAG:
                        step(before)
                if i >= LAG + 1 and (i - LAG - 1) % 2 == 0 and (i - LAG - 1) // 2 < PASSING:
                    load_again(first_turned[(i - LAG - 1) // 2])
            with sp.Fori(0, TURNS) as turn:
                for i in range(LAG, LAG + TURN):
                    step(i, turn)
            for i in range(LAG + TURNS * TURN, GROUPS + LAG):
                step(i)
            for g in range(G - 1):
                sp.wait_ge(rows_ready, U * (g + 1))
                sp.dma_start(rows(out, g), out_rows[g].rearrange("p (u c) -> p u c", u=U)).then_inc(out_stored, 16)
            last_rows = out_rows[G - 1].rearrange("p (u c) -> p u c", u=U)
            sp.wait_ge(rows_ready, U * G - U // 2)
            sp.dma_start(rows(out, G - 1)[:, :U // 2], last_rows[:, :U // 2]).then_inc(out_stored, 16)
            sp.wait_ge(rows_ready_dve, U // 2)
            sp.dma_start(rows(out, G - 1)[:, U // 2:], last_rows[:, U // 2:]).then_inc(out_stored, 16)
            sp.wait_ge(out_stored, 16 * (G + 1))

        @block.gpsimd
        def _(pool):
            pool.memset(ident[:], 0.0).then_inc(ident_zeroed, 1)
            pool.wait_ge(ident_zeroed, 1)
            pool.affine_select(out=ident[:], in_=ident[:], compare_op=ALU.not_equal, fill=1.0, base=0,
                               pattern=[[-1, P]], channel_multiplier=1).then_inc(ident_ready, 1)
            pool.dma_start(evals_sb[:, 0], evals.rearrange("(k p) -> k p", p=P)).then_inc(spectrum_loaded, 16)
            for b in range(B):
                pool.dma_start(evals_sb[b * U:(b + 1) * U, 1].rearrange("k (b c) -> k b c", c=Q),
                               evals[b * W:(b + 1) * W].rearrange("(b k c) -> k b c", k=U, c=Q)
                               ).then_inc(spectrum_loaded, 16)
            pool.dma_start(t_sb[:], t.rearrange("(a b) -> a b", a=1).to_broadcast([KT, 1])).then_inc(spectrum_loaded, 16)

            def split_low(n, turn=0):
                pool.wait_ge(a_hi_ready, turn * TT + (n + 1))
                pool.tensor_tensor(a_lo[:, n % BUFFERS], adj_tile(n), a_hi[:, n % BUFFERS].bitcast(F32),
                                   ALU.subtract).then_inc(a_lo_ready_pool, 1)

            with pool.Fori(0, TURNS) as turn:
                for n in range(LEAD, LEAD + TT):
                    split_low(n, turn)
            for n in range(LEAD + TURNS * TT, TILES):
                split_low(n)
            for m in range(TAIL, TILES):
                if on_pool(m):
                    pool.wait_ge(at_hi_ready, hi_count(m))
                    pool.tensor_tensor(at_lo_tile(m), turned_tile(m), at_hi_tile(m).bitcast(F32),
                                       ALU.subtract).then_inc(at_lo_ready_pool, 1)

        @block.scalar
        def _(act):
            def split_x_high(g):
                act.wait_ge(x_loaded[g], 16)
                act.activation(x_hi[:, g], acc[:, g].rearrange("p (u c) -> p u c", u=U), ACT.Copy).then_inc(x_hi_ready, 1)

            def split_high(n, turn=0):
                i = n // U
                if n % U == 0:
                    loaded = passing_loaded if turned(i) else kept_loaded
                    act.wait_ge(loaded[slot(i)], turn * (16 * uses_in_turn(i)) + 16 * use(i))
                if n >= BUFFERS:
                    act.wait_ge(first_done, turn * TT + (n + 1 - BUFFERS))
                act.activation(a_hi[:, n % BUFFERS], adj_tile(n), ACT.Copy).then_inc(a_hi_ready, 1)

            def split_high_transposed(m, turn=0):
                if turned(m // U):
                    act.wait_ge(at_turned, turn * own_in_turn(m) + own(m))
                    act.wait_ge(second_done, turn * TT + (m + 1 - (2 * BUFFERS if m >= TAIL else BUFFERS)))
                else:
                    act.wait_ge(at_transposed, turn * own_in_turn(m) + own(m))
                if TAIL <= m < TAIL + BUFFERS:
                    act.wait_ge(first_done, m + 1 - TAIL + TILES - BUFFERS)
                act.activation(at_hi_tile(m), at_tile(m), ACT.Copy).then_inc(at_hi_ready, 1)

            def copy_y(b, turn=0):
                act.wait_ge(first_done, turn * TT + G * U * (b + 1))
                if b >= 1:
                    act.wait_ge(s_ready, turn * 4 + 2 * b)
                act.activation(y_sb[:, 0], y_ps[:, b % 2], ACT.Copy).then_inc(y_copied, 1)
                act.activation(y_sb[:, 1].rearrange("p (k b c) -> p k b c", k=U, c=Q),
                               y_ps[:, b % 2].rearrange("p (b k c) -> p k b c", k=U, c=Q), ACT.Copy).then_inc(y_copied, 1)

            def split_s_high(b, order, turn=0):
                act.wait_ge(s_scaled, turn * 4 + (2 * b + order + 1))
                if b >= 2:
                    act.wait_ge(second_done, turn * TT + G * U * (b - 1))
                act.activation(s_hi[:, b % 2, order], y_sb[:, order].rearrange("p (u c) -> p u c", u=U), ACT.Copy).then_inc(s_hi_ready, 1)

            def deviation(g):
                act.wait_ge(mean_var_ready, g + 1)
                if g >= 2:
                    act.wait_ge(rstd_ready, g - 1)
                act.activation(std[:, g % 2], mean_var[:, g % 2, :, 1], ACT.Sqrt, bias=eps_sb[:]).then_inc(std_ready, 1)

            def normalise(g, u):
                act.wait_ge(shift_ready, g + 1)
                act.activation(out_rows[g][:, u * C:(u + 1) * C], rows_ps(g, u), ACT.Identity,
                               scale=rstd[:, g % 2, u:u + 1], bias=shift[:, g % 2, u:u + 1]).then_inc(rows_ready, 1)

            def step(i, turn=0):
                j = i - LAG
                for u in range(U):
                    if i < GROUPS:
                        split_high(i * U + u, turn)
                    if u == 2 and i + 1 < G:
                        split_x_high(i + 1)
                    for b, order in s_made(i):
                        if order == 0 and u == 2:
                            copy_y(b, turn)
                    if j >= 0:
                        for m in hi_order(j)[u]:
                            split_high_transposed(m, turn)
                    for b, order in s_made(i - 1):
                        if u == 1:
                            split_s_high(b, order, turn)
                    if u == 2 and finished(i) >= 1:
                        deviation(finished(i) - 1)
                    if u == 3 and finished(i) >= 1:
                        normalise(finished(i) - 1, 0)
                    if u < 3 and finished(i) >= 2:
                        normalise(finished(i) - 2, u + 1)

            split_x_high(0)
            for g in range(G):
                step(g)
                act.wait_ge(x_transposed, g + 1)
                act.wait_ge(x_lo_ready, g + 1)
                act.activation(acc[:, g], at_ps[:, g % U], ACT.Copy).then_inc(acc_written, 1)
                if g == G - 2:
                    act.wait_ge(spectrum_loaded, 16 * (B + 2))
                    act.wait_ge(t_ready, 1)
                    act.activation(coef_rows[:], evals_sb[:], ACT.Exp, scale=neg_t[:]).then_inc(coef_rows_ready, 1)
            step(G)
            with act.Fori(0, TURNS) as turn:
                for i in range(LAG, LAG + TURN):
                    step(i, turn)
            act.wait_ge(eps_ready, 1)
            for i in range(LAG + TURNS * TURN, GROUPS + LAG):
                step(i)
            for u in range(1, U):
                normalise(G - 3, u)
            for g in (G - 2, G - 1):
                deviation(g)
                for u in range(U if g < G - 1 else U // 2):
                    normalise(g, u)

        @block.vector
        def _(dve):
            dve.memset(eps_sb[:], EPS).then_inc(eps_ready, 1)

            def split_low(n):
                dve.wait_ge(a_hi_ready, n + 1)
                dve.tensor_tensor(a_lo[:, n % BUFFERS], adj_tile(n), a_hi[:, n % BUFFERS].bitcast(F32),
                                  ALU.subtract).then_inc(a_lo_ready_dve, 1)

            def split_x_low(g):
                dve.wait_ge(x_hi_ready, g + 1)
                dve.tensor_tensor(x_lo[:, g], acc[:, g].rearrange("p (u c) -> p u c", u=U),
                                  x_hi[:, g].bitcast(F32), ALU.subtract).then_inc(x_lo_ready, 1)

            def turn_tile(m, turn=0):
                j = m // U
                if m % U == 0:
                    dve.wait_ge(again_loaded[slot(j)],
                                turn * (16 * U * uses_in_turn(j)) + 16 * U * use(j))
                if not on_pool(m):
                    dve.wait_ge(at_lo_ready_dve, turn * TT + (m - U + 1))
                elif m < TAIL + 4 * U:
                    dve.wait_ge(first_done, TILES - (2 * U if m < TAIL + 2 * U else 0))
                else:
                    dve.wait_ge(at_lo_ready_pool, pool_count(m - 4 * U))
                k = m % U
                dve.transpose(at_tile(m).rearrange("p (m r) -> p m r", r=Q),
                              again[:, slot(j), :, k * Q:(k + 1) * Q]).then_inc(at_turned, 1)

            def split_low_transposed(m, turn=0):
                dve.wait_ge(at_hi_ready, turn * TT + hi_count(m))
                dve.tensor_tensor(at_lo_tile(m), at_tile(m),
                                  at_hi_tile(m).bitcast(F32), ALU.subtract).then_inc(at_lo_ready_dve, 1)

            def accumulate(j, turn=0):
                dve.wait_ge(second_done, turn * TT + U * (j + 1))
                if j == GROUPS - 1:
                    for half in (slice(0, W // 2), slice(W // 2, W)):
                        dve.tensor_tensor(acc[:, j % G, half], o_ps[:, j % 2, half], acc[:, j % G, half],
                                          ALU.add).then_inc(acc_written, 1)
                    return
                dve.tensor_tensor(acc[:, j % G], o_ps[:, j % 2], acc[:, j % G], ALU.add).then_inc(acc_written, 1)

            def scale_s(b, order, turn=0):
                dve.wait_ge(y_transposed, turn * 4 + (2 * b + order + 1))
                c = coef[:, order, bass.ds(turn * (2 * U) + b * U, U)].unsqueeze(2).to_broadcast([P, U, C])
                dve.tensor_tensor(y_sb[:, order].rearrange("p (u c) -> p u c", u=U),
                                  y_ps[:, b % 2].rearrange("p (u c) -> p u c", u=U), c, ALU.mult).then_inc(s_scaled, 1)

            def split_s_low(b, order, turn=0):
                dve.wait_ge(s_hi_ready, turn * 4 + (2 * b + order + 1))
                dve.tensor_tensor(s_lo[:, b % 2, order], y_sb[:, order].rearrange("p (u c) -> p u c", u=U),
                                  s_hi[:, b % 2, order].bitcast(F32), ALU.subtract).then_inc(s_ready, 1)

            def statistics(g):
                dve.wait_ge(rows_transposed, g + 1)
                for u in range(U):
                    if g == G - 1 and u == U // 2:
                        dve.wait_ge(rows_transposed, G + 1)
                    dve.bn_stats(stats[:, u], rows_ps(g, u)).then_inc(stats_ready, 1)
                dve.wait_ge(stats_ready, U * (g + 1))
                if g >= 2:
                    dve.wait_ge(std_ready, g - 1)
                for u in range(U):
                    last = dve.bn_aggr(mean_var[:, g % 2, u], stats[:, u])
                last.then_inc(mean_var_ready, 1)

            def shift_and_scale(g):
                dve.wait_ge(std_ready, g + 1)
                if g >= 2:
                    dve.wait_ge(rows_ready, U * (g - 1))
                dve.reciprocal(rstd[:, g % 2], std[:, g % 2]).then_inc(rstd_ready, 1)
                dve.wait_ge(rstd_ready, g + 1)
                dve.scalar_tensor_tensor(shift[:, g % 2], mean_var[:, g % 2, :, 0], -1.0, rstd[:, g % 2],
                                         ALU.mult, ALU.mult).then_inc(shift_ready, 1)

            def tile_step(i, u, turn=0):
                j = i - LAG
                m = j * U + u
                for b, order in s_made(i):
                    if u == 3:
                        scale_s(b, order, turn)
                for b, order in s_made(i - 1):
                    if u == 0:
                        split_s_low(b, order, turn)
                if u == 1 and finished(i) >= 1:
                    shift_and_scale(finished(i) - 1)
                if u == 3 and finished(i) >= 0:
                    statistics(finished(i))
                ahead = 4 if m + 4 < TAIL + U else 8
                if j >= 0 and m + ahead < TILES and turned((m + ahead) // U):
                    turn_tile(m + ahead, turn)
                if j >= 0 and m + 2 < TILES and not on_pool(m + 2):
                    split_low_transposed(m + 2, turn)

            def step(i, turn=0):
                for u in range(1, U):
                    tile_step(i, u, turn)
                if i < GROUPS + LAG - 1:
                    tile_step(i + 1, 0, turn)
                if i >= LAG:
                    accumulate(i - LAG, turn)

            split_x_low(0)
            for n in range(LEAD):
                split_low(n)
                if n % U == 2 and n // U + 1 < G:
                    split_x_low(n // U + 1)
                if n == (G - 2) * U:
                    dve.wait_ge(spectrum_loaded, 16 * (B + 2))
                    dve.tensor_scalar(neg_t[:], t_sb[:], T_MIN, -1.0, ALU.max, ALU.mult).then_inc(t_ready, 1)
                if n == (G - 1) * U:
                    dve.wait_ge(coef_transposed, 1)
                    dve.tensor_copy(coef[:].rearrange("p o k -> p (o k)"), o_ps[:, 0, 0:2 * KT]).then_inc(coef_ready, 1)
            dve.wait_ge(coef_ready, 1)
            for u in range(U):
                tile_step(G, u)
            split_low_transposed(0)
            split_low_transposed(1)
            tile_step(LAG, 0)
            with dve.Fori(0, TURNS) as turn:
                for i in range(LAG, LAG + TURN):
                    step(i, turn)
            for i in range(LAG + TURNS * TURN, GROUPS + LAG):
                step(i)
            tile_step(GROUPS + LAG, 0)
            shift_and_scale(G - 2)
            statistics(G - 1)
            shift_and_scale(G - 1)
            dve.wait_ge(shift_ready, G)
            for u in range(U // 2, U):
                dve.tensor_scalar(out_rows[G - 1][:, u * C:(u + 1) * C], rows_ps(G - 1, u),
                                  rstd[:, (G - 1) % 2, u:u + 1], shift[:, (G - 1) % 2, u:u + 1],
                                  ALU.mult, ALU.add).then_inc(rows_ready_dve, 1)

        @block.tensor
        def _(pe):
            pe.wait_ge(ident_ready, 1)

            def transpose_tiles(m):
                for u in range(U):
                    last = pe.transpose(at_ps[:, m % U, u * P:(u + 1) * P],
                                        kept[:, slot(m // U), u, m % U * P:(m % U + 1) * P], ident[:])
                last.then_inc(at_transposed, 1)

            def first_product(n, turn=0):
                i, y = n // U, y_ps[:, n // U // G % 2]
                g, u = i % G, n % U
                first, end = g == 0 and u == 0, g == G - 1 and u == U - 1
                hi, lo = a_hi[:, n % BUFFERS], a_lo[:, n % BUFFERS]
                pe.wait_ge(a_hi_ready, turn * TT + (n + 1))
                if first and i // G >= 2:
                    pe.wait_ge(s_scaled, turn * 4 + 2 * (i // G - 1))
                pe.matmul(y, x_hi[:, g, u], hi, start=first, stop=False)
                pe.matmul(y, x_lo[:, g, u], hi, start=False, stop=False)
                if n < LEAD:
                    pe.wait_ge(a_lo_ready_dve, n + 1)
                else:
                    pe.wait_ge(a_lo_ready_pool, turn * TT + (n + 1 - LEAD))
                pe.matmul(y, x_hi[:, g, u], lo, start=False, stop=end).then_inc(first_done, 1)

            def second_product(m, turn=0):
                j, k, o = m // U, m % U, o_ps[:, m // U % 2]
                order = int(turned(j))
                s_h, s_l = s_hi[:, j // G % 2, order, k], s_lo[:, j // G % 2, order, k]
                hi, lo = at_hi_tile(m), at_lo_tile(m)
                if k == 0:
                    if j % G < 2:
                        pe.wait_ge(s_ready, turn * 4 + (2 * (j // G) + j % G + 1))
                    pe.wait_ge(acc_written, turn * TURN + (G + j - 1))
                pe.wait_ge(at_hi_ready, turn * TT + hi_count(m))
                pe.matmul(o, s_h, hi, start=k == 0, stop=False)
                pe.matmul(o, s_l, hi, start=False, stop=False)
                if on_pool(m):
                    pe.wait_ge(at_lo_ready_pool, pool_count(m))
                elif m >= TAIL:
                    pe.wait_ge(at_lo_ready_dve, m + 1 - pool_count(m))
                else:
                    pe.wait_ge(at_lo_ready_dve, turn * TT + (m + 1))
                pe.matmul(o, s_h, lo, start=False, stop=k == U - 1).then_inc(second_done, 1)

            def transpose_y(b, order, turn=0):
                pe.wait_ge(y_copied, turn * 4 + 2 * (b + 1))
                if order == 1:
                    pe.wait_ge(s_scaled, turn * 4 + (2 * b + 1))
                for k in range(U):
                    last = pe.transpose(y_ps[:, b % 2, k * C:(k + 1) * C], y_sb[:, order, k * P:(k + 1) * P], ident[:])
                last.then_inc(y_transposed, 1)

            def transpose_rows(g):
                pe.wait_ge(acc_written, GROUPS + g + 1)
                if g >= 2:
                    pe.wait_ge(rows_ready, U * (g - 1))
                for u in range(U):
                    if g == G - 1 and u == U // 2:
                        last.then_inc(rows_transposed, 1)
                        pe.wait_ge(acc_written, GROUPS + G + 1)
                    last = pe.transpose(rows_ps(g, u), acc[:, g, u * P:(u + 1) * P], ident[:])
                last.then_inc(rows_transposed, 1)

            def transpose_x(g):
                pe.wait_ge(x_loaded[g], 16)
                if g >= U:
                    pe.wait_ge(acc_written, g - U + 1)
                for u in range(U):
                    last = pe.transpose(at_ps[:, g % U, u * P:(u + 1) * P], acc[:, g, u * C:(u + 1) * C], ident[:])
                last.then_inc(x_transposed, 1)

            def step(i, turn=0):
                j = i - LAG
                for u in range(U):
                    m = j * U + u
                    if j >= 0 and m + 3 < TILES and not turned((m + 3) // U):
                        transpose_tiles(m + 3)
                    if i < GROUPS:
                        first_product(i * U + u, turn)
                    if u == 2 and i + 1 < G:
                        transpose_x(i + 1)
                    for b, order in s_made(i):
                        if u == 1:
                            transpose_y(b, order, turn)
                    if j >= 0:
                        second_product(m, turn)
                    if u == 1 and finished(i) >= 0:
                        transpose_rows(finished(i))

            transpose_x(0)
            for g in range(G):
                pe.wait_ge(x_lo_ready, g + 1)
                step(g)
                if g == G - 2:
                    pe.wait_ge(coef_rows_ready, 1)
                    for order in range(2):
                        last = pe.transpose(o_ps[:, 0, order * KT:(order + 1) * KT], coef_rows[:, order],
                                            ident[0:KT, 0:KT])
                    last.then_inc(coef_transposed, 1)
            step(G)
            pe.wait_ge(acc_written, G)
            for m in range(3):
                transpose_tiles(m)
            with pe.Fori(0, TURNS) as turn:
                for i in range(LAG, LAG + TURN):
                    step(i, turn)
            for i in range(LAG + TURNS * TURN, GROUPS + LAG):
                step(i)
            transpose_rows(G - 1)


def kernel(x, adj, L0_gnn_evals, L0_gnn_t):
    import numpy as np
    from concourse import bacc
    from concourse.bass_utils import run_bass_kernel_spmd

    nc = bacc.Bacc("TRN2", target_bir_lowering=False, num_devices=1)
    given = {"x": x, "adj": adj, "evals": L0_gnn_evals, "t": L0_gnn_t}
    arrays = {name: np.ascontiguousarray(a) for name, a in given.items()}
    ins = [nc.dram_tensor(name, a.shape, mybir.dt.from_np(a.dtype), kind="ExternalInput").ap()
           for name, a in arrays.items()]
    out = nc.dram_tensor("out", arrays["x"].shape, F32, kind="ExternalOutput").ap()
    heat_layernorm(nc, *ins, out)
    return run_bass_kernel_spmd(nc, [arrays], core_ids=[0]).results[0]["out"]
```
